# Optimizing a Trainium2 kernel written in Bass

```python
import numpy as np
import jax
import jax.numpy as jnp

def _softmax(x, axis=-1):
    return jax.nn.softmax(x, axis=axis)

def _gelu(x):
    return jax.nn.gelu(x, approximate=True)

def _silu(x):
    return jax.nn.silu(x)

def _sigmoid(x):
    return jax.nn.sigmoid(x)

def _layernorm(x, axis=-1, eps=1e-05):
    m = jnp.mean(x, axis=axis, keepdims=True)
    v = jnp.var(x, axis=axis, keepdims=True)
    return (x - m) / jnp.sqrt(v + eps)

def _scatter_add(tgt, idx, src, axis=0):
    return tgt.at[idx].add(src)

def _segment_sum(src, seg, n):
    return jax.ops.segment_sum(src, seg, n)
kernel_name = 'mk_sandwich_d1_jaxref_r8_b15655'

def setup_inputs(seed: int=0):
    np.random.seed(seed)
    _w = jnp.asarray

    def _L0_attn_setup():
        import jax, jax.numpy as jnp
        import numpy as np
        import math
        B, S, E = (2, 256, 128)
        H, DC, DR = (16, 32, 128)
        HD = E // H

        def _linear_params(key, din, dout):
            k1, k2 = jax.random.split(key)
            bound = 1.0 / math.sqrt(din)
            w = jax.random.uniform(k1, (din, dout), minval=-bound, maxval=bound, dtype=jnp.float32)
            b = jax.random.uniform(k2, (dout,), minval=-bound, maxval=bound, dtype=jnp.float32)
            return (w, b)

        def _gelu(x):
            return jax.nn.gelu(x, approximate=False)

        def _rope_cos_sin(seq_len, d_rope):
            inv_freq = 1.0 / 10000.0 ** (jnp.arange(0, d_rope, 2, dtype=jnp.float32) / d_rope)
            t = jnp.arange(seq_len, dtype=jnp.float32)
            freqs = t[:, None] * inv_freq[None, :]
            emb = jnp.concatenate([freqs, freqs], axis=-1)
            return (jnp.cos(emb), jnp.sin(emb))

        def _apply_rope(x, cos, sin):
            d = x.shape[-1]
            x1, x2 = (x[..., :d // 2], x[..., d // 2:])
            rot = jnp.concatenate([-x2, x1], axis=-1)
            return x * cos + rot * sin
        key = jax.random.key(seed)
        ks = jax.random.split(key, 10)
        x = jax.random.normal(ks[0], (B, S, E), dtype=jnp.float32)
        wq, bq = _linear_params(ks[1], E, DC)
        wqc, bqc = _linear_params(ks[2], DC, E - DR)
        wqr, bqr = _linear_params(ks[3], E, DR)
        wkv, bkv = _linear_params(ks[4], E, DC)
        wkr, bkr = _linear_params(ks[5], E, DR)
        wkc, bkc = _linear_params(ks[6], DC, E - DR)
        wv, bv = _linear_params(ks[7], DC, E)
        wo, bo = _linear_params(ks[8], E, E)
        return dict(x=x, wq=wq, bq=bq, wqc=wqc, bqc=bqc, wqr=wqr, bqr=bqr, wkv=wkv, bkv=bkv, wkr=wkr, bkr=bkr, wkc=wkc, bkc=bkc, wv=wv, bv=bv, wo=wo, bo=bo)
    _L0_attn_in = _L0_attn_setup()

    def _L0_ffn_setup():
        import jax, jax.numpy as jnp
        import numpy as np
        DIM = 128
        DEPTH = 6
        HEADS = 16
        DIM_HEAD = 64
        WINDOW = 32
        INNER = HEADS * DIM_HEAD
        DIM_INNER = int(DIM * 4 * 2 / 3)
        QK_SCALE = 8.0

        def shift_tokens(t):
            a, s = jnp.split(t, 2, -1)
            s = jnp.pad(s, ((0, 0), (1, 0), (0, 0)))[:, :-1]
            return jnp.concatenate([a, s], -1)

        def l2norm(t):
            return t / jnp.maximum(jnp.linalg.norm(t, axis=-1, keepdims=True), 1e-12)

        def rotate_half(x):
            x1, x2 = jnp.split(x, 2, -1)
            return jnp.concatenate([-x2, x1], -1)

        def rotary_tables(n):
            half = jnp.arange(0, DIM_HEAD, 2, dtype=jnp.float32)
            inv_freq = 1.0 / 10000.0 ** (half / DIM_HEAD)
            t = jnp.arange(n, dtype=jnp.float32)
            freqs = t[:, None] * inv_freq[None, :]
            freqs = jnp.concatenate([freqs, freqs], -1)
            base_scale = (half + 0.4 * DIM_HEAD) / (1.4 * DIM_HEAD)
            power = (t - n // 2) / (WINDOW // 2)
            scale = base_scale[None, :] ** power[:, None]
            scale = jnp.concatenate([scale, scale], -1)
            return (freqs, scale)

        def local_attention(q, k, v):
            b, h, n, d = q.shape
            w = WINDOW
            nw = n // w
            bq = q.reshape(b, h, nw, w, d)
            bk = k.reshape(b, h, nw, w, d)
            bv = v.reshape(b, h, nw, w, d)

            def look(t):
                p = jnp.pad(t, ((0, 0), (0, 0), (1, 0), (0, 0), (0, 0)))
                return jnp.concatenate([p[:, :, :nw], p[:, :, 1:]], axis=3)
            bk2, bv2 = (look(bk), look(bv))
            seq = jnp.arange(n).reshape(nw, w)
            seq_p = jnp.pad(seq, ((1, 0), (0, 0)), constant_values=-1)
            jt = jnp.concatenate([seq_p[:nw], seq_p[1:]], axis=1)
            it = seq[:, :, None]
            jb = jt[:, None, :]
            mask = (it < jb) | (it > jb + w) | (jb == -1)
            sim = jnp.einsum('bhwie,bhwje->bhwij', bq, bk2) * QK_SCALE
            sim = jnp.where(mask, -jnp.finfo(sim.dtype).max, sim)
            attn = jax.nn.softmax(sim, -1)
            out = jnp.einsum('bhwij,bhwje->bhwie', attn, bv2)
            return out.reshape(b, h, n, d)

        def attn_layer(x, Wqkv, qs, ksc, Wo):
            b, n, _ = x.shape
            qkv = x @ Wqkv
            q, k, v = jnp.split(qkv, 3, -1)
            sh = lambda t: t.reshape(b, n, HEADS, DIM_HEAD).transpose(0, 2, 1, 3)
            q, k, v = (sh(q), sh(k), sh(v))
            q = l2norm(q) * qs
            k = l2norm(k) * ksc
            freqs, scale = rotary_tables(n)
            cos, sin = (jnp.cos(freqs), jnp.sin(freqs))
            q = q * cos * scale + rotate_half(q) * sin * scale
            inv = 1.0 / scale
            k = k * cos * inv + rotate_half(k) * sin * inv
            out = local_attention(q, k, v)
            out = out.transpose(0, 2, 1, 3).reshape(b, n, INNER)
            return out @ Wo

        def ffn_layer(x, g, bln, W1, b1, W2, b2):
            mu = x.mean(-1, keepdims=True)
            var = ((x - mu) ** 2).mean(-1, keepdims=True)
            xn = (x - mu) / jnp.sqrt(var + 1e-05) * g + bln
            hg = xn @ W1 + b1
            a, gate = jnp.split(hg, 2, -1)
            return a * jax.nn.gelu(gate, approximate=False) @ W2 + b2
        key = jax.random.key(seed)
        ks = jax.random.split(key, 8)
        B, N = (2, 256)
        init = lambda k, shape: jax.random.normal(k, shape, jnp.float32) * 0.02
        return {'x': jax.random.normal(ks[0], (B, N, DIM), jnp.float32), 'Wqkv': init(ks[1], (DEPTH, DIM, 3 * INNER)), 'q_scale': jnp.ones((DEPTH, DIM_HEAD), jnp.float32), 'k_scale': jnp.ones((DEPTH, DIM_HEAD), jnp.float32), 'Wo': init(ks[2], (DEPTH, INNER, DIM)), 'ln_g': jnp.ones((DEPTH, DIM), jnp.float32), 'ln_b': jnp.zeros((DEPTH, DIM), jnp.float32), 'W1': init(ks[3], (DEPTH, DIM, 2 * DIM_INNER)), 'b1': jnp.zeros((DEPTH, 2 * DIM_INNER), jnp.float32), 'W2': init(ks[4], (DEPTH, DIM_INNER, DIM)), 'b2': jnp.zeros((DEPTH, DIM), jnp.float32)}
    _L0_ffn_in = _L0_ffn_setup()
    _d = {'L0_attn_x': _L0_attn_in['x'], 'L0_attn_wq': _L0_attn_in['wq'], 'L0_attn_bq': _L0_attn_in['bq'], 'L0_attn_wqc': _L0_attn_in['wqc'], 'L0_attn_bqc': _L0_attn_in['bqc'], 'L0_attn_wqr': _L0_attn_in['wqr'], 'L0_attn_bqr': _L0_attn_in['bqr'], 'L0_attn_wkv': _L0_attn_in['wkv'], 'L0_attn_bkv': _L0_attn_in['bkv'], 'L0_attn_wkr': _L0_attn_in['wkr'], 'L0_attn_bkr': _L0_attn_in['bkr'], 'L0_attn_wkc': _L0_attn_in['wkc'], 'L0_attn_bkc': _L0_attn_in['bkc'], 'L0_attn_wv': _L0_attn_in['wv'], 'L0_attn_bv': _L0_attn_in['bv'], 'L0_attn_wo': _L0_attn_in['wo'], 'L0_attn_bo': _L0_attn_in['bo'], 'L0_ffn_Wqkv': _L0_ffn_in['Wqkv'], 'L0_ffn_q_scale': _L0_ffn_in['q_scale'], 'L0_ffn_k_scale': _L0_ffn_in['k_scale'], 'L0_ffn_Wo': _L0_ffn_in['Wo'], 'L0_ffn_ln_g': _L0_ffn_in['ln_g'], 'L0_ffn_ln_b': _L0_ffn_in['ln_b'], 'L0_ffn_W1': _L0_ffn_in['W1'], 'L0_ffn_b1': _L0_ffn_in['b1'], 'L0_ffn_W2': _L0_ffn_in['W2'], 'L0_ffn_b2': _L0_ffn_in['b2']}
    _x0 = _d['L0_attn_x']
    _d['L0_attn_x'] = jax.random.normal(jax.random.fold_in(jax.random.key(seed), 1), (4, 512, 128), dtype=_x0.dtype)
    del _x0
    return _d

def reference(L0_attn_x, L0_attn_wq, L0_attn_bq, L0_attn_wqc, L0_attn_bqc, L0_attn_wqr, L0_attn_bqr, L0_attn_wkv, L0_attn_bkv, L0_attn_wkr, L0_attn_bkr, L0_attn_wkc, L0_attn_bkc, L0_attn_wv, L0_attn_bv, L0_attn_wo, L0_attn_bo, L0_ffn_Wqkv, L0_ffn_q_scale, L0_ffn_k_scale, L0_ffn_Wo, L0_ffn_ln_g, L0_ffn_ln_b, L0_ffn_W1, L0_ffn_b1, L0_ffn_W2, L0_ffn_b2):

    def _L0_attn_ref(x, wq, bq, wqc, bqc, wqr, bqr, wkv, bkv, wkr, bkr, wkc, bkc, wv, bv, wo, bo):
        import jax, jax.numpy as jnp
        import numpy as np
        import math
        B, S, E = (2, 256, 128)
        H, DC, DR = (16, 32, 128)
        HD = E // H

        def _linear_params(key, din, dout):
            k1, k2 = jax.random.split(key)
            bound = 1.0 / math.sqrt(din)
            w = jax.random.uniform(k1, (din, dout), minval=-bound, maxval=bound, dtype=jnp.float32)
            b = jax.random.uniform(k2, (dout,), minval=-bound, maxval=bound, dtype=jnp.float32)
            return (w, b)

        def _gelu(x):
            return jax.nn.gelu(x, approximate=False)

        def _rope_cos_sin(seq_len, d_rope):
            inv_freq = 1.0 / 10000.0 ** (jnp.arange(0, d_rope, 2, dtype=jnp.float32) / d_rope)
            t = jnp.arange(seq_len, dtype=jnp.float32)
            freqs = t[:, None] * inv_freq[None, :]
            emb = jnp.concatenate([freqs, freqs], axis=-1)
            return (jnp.cos(emb), jnp.sin(emb))

        def _apply_rope(x, cos, sin):
            d = x.shape[-1]
            x1, x2 = (x[..., :d // 2], x[..., d // 2:])
            rot = jnp.concatenate([-x2, x1], axis=-1)
            return x * cos + rot * sin
        b, s, _ = x.shape
        cq = _gelu(x @ wq + bq)
        q_c = cq @ wqc + bqc
        q_r = x @ wqr + bqr
        ckv = _gelu(x @ wkv + bkv)
        k_r = x @ wkr + bkr
        k_c = ckv @ wkc + bkc
        v = (ckv @ wv + bv).reshape(b, s, H, HD).transpose(0, 2, 1, 3)
        cos, sin = _rope_cos_sin(s, DR)
        q_r = _apply_rope(q_r, cos, sin)
        k_r = _apply_rope(k_r, cos, sin)
        q = _gelu(jnp.concatenate([q_c, q_r], axis=-1)).reshape(b, s, H, HD).transpose(0, 2, 1, 3)
        k = _gelu(jnp.concatenate([k_c, k_r], axis=-1)).reshape(b, s, H, HD).transpose(0, 2, 1, 3)
        scale = 1.0 / math.sqrt(HD)
        scores = jnp.einsum('bhqd,bhkd->bhqk', q, k) * scale
        causal = jnp.triu(jnp.ones((s, s), dtype=bool), k=1)
        scores = jnp.where(causal[None, None], -jnp.inf, scores)
        attn = jax.nn.softmax(scores, axis=-1)
        out = jnp.einsum('bhqk,bhkd->bhqd', attn, v)
        out = out.transpose(0, 2, 1, 3).reshape(b, s, E)
        return out @ wo + bo

    def _L0_ffn_ref(x, Wqkv, q_scale, k_scale, Wo, ln_g, ln_b, W1, b1, W2, b2):
        import jax, jax.numpy as jnp
        import numpy as np
        DIM = 128
        DEPTH = 6
        HEADS = 16
        DIM_HEAD = 64
        WINDOW = 32
        INNER = HEADS * DIM_HEAD
        DIM_INNER = int(DIM * 4 * 2 / 3)
        QK_SCALE = 8.0

        def shift_tokens(t):
            a, s = jnp.split(t, 2, -1)
            s = jnp.pad(s, ((0, 0), (1, 0), (0, 0)))[:, :-1]
            return jnp.concatenate([a, s], -1)

        def l2norm(t):
            return t / jnp.maximum(jnp.linalg.norm(t, axis=-1, keepdims=True), 1e-12)

        def rotate_half(x):
            x1, x2 = jnp.split(x, 2, -1)
            return jnp.concatenate([-x2, x1], -1)

        def rotary_tables(n):
            half = jnp.arange(0, DIM_HEAD, 2, dtype=jnp.float32)
            inv_freq = 1.0 / 10000.0 ** (half / DIM_HEAD)
            t = jnp.arange(n, dtype=jnp.float32)
            freqs = t[:, None] * inv_freq[None, :]
            freqs = jnp.concatenate([freqs, freqs], -1)
            base_scale = (half + 0.4 * DIM_HEAD) / (1.4 * DIM_HEAD)
            power = (t - n // 2) / (WINDOW // 2)
            scale = base_scale[None, :] ** power[:, None]
            scale = jnp.concatenate([scale, scale], -1)
            return (freqs, scale)

        def local_attention(q, k, v):
            b, h, n, d = q.shape
            w = WINDOW
            nw = n // w
            bq = q.reshape(b, h, nw, w, d)
            bk = k.reshape(b, h, nw, w, d)
            bv = v.reshape(b, h, nw, w, d)

            def look(t):
                p = jnp.pad(t, ((0, 0), (0, 0), (1, 0), (0, 0), (0, 0)))
                return jnp.concatenate([p[:, :, :nw], p[:, :, 1:]], axis=3)
            bk2, bv2 = (look(bk), look(bv))
            seq = jnp.arange(n).reshape(nw, w)
            seq_p = jnp.pad(seq, ((1, 0), (0, 0)), constant_values=-1)
            jt = jnp.concatenate([seq_p[:nw], seq_p[1:]], axis=1)
            it = seq[:, :, None]
            jb = jt[:, None, :]
            mask = (it < jb) | (it > jb + w) | (jb == -1)
            sim = jnp.einsum('bhwie,bhwje->bhwij', bq, bk2) * QK_SCALE
            sim = jnp.where(mask, -jnp.finfo(sim.dtype).max, sim)
            attn = jax.nn.softmax(sim, -1)
            out = jnp.einsum('bhwij,bhwje->bhwie', attn, bv2)
            return out.reshape(b, h, n, d)

        def attn_layer(x, Wqkv, qs, ksc, Wo):
            b, n, _ = x.shape
            qkv = x @ Wqkv
            q, k, v = jnp.split(qkv, 3, -1)
            sh = lambda t: t.reshape(b, n, HEADS, DIM_HEAD).transpose(0, 2, 1, 3)
            q, k, v = (sh(q), sh(k), sh(v))
            q = l2norm(q) * qs
            k = l2norm(k) * ksc
            freqs, scale = rotary_tables(n)
            cos, sin = (jnp.cos(freqs), jnp.sin(freqs))
            q = q * cos * scale + rotate_half(q) * sin * scale
            inv = 1.0 / scale
            k = k * cos * inv + rotate_half(k) * sin * inv
            out = local_attention(q, k, v)
            out = out.transpose(0, 2, 1, 3).reshape(b, n, INNER)
            return out @ Wo

        def ffn_layer(x, g, bln, W1, b1, W2, b2):
            mu = x.mean(-1, keepdims=True)
            var = ((x - mu) ** 2).mean(-1, keepdims=True)
            xn = (x - mu) / jnp.sqrt(var + 1e-05) * g + bln
            hg = xn @ W1 + b1
            a, gate = jnp.split(hg, 2, -1)
            return a * jax.nn.gelu(gate, approximate=False) @ W2 + b2
        for i in range(DEPTH):
            x = attn_layer(shift_tokens(x), Wqkv[i], q_scale[i], k_scale[i], Wo[i]) + x
            x = ffn_layer(shift_tokens(x), ln_g[i], ln_b[i], W1[i], b1[i], W2[i], b2[i]) + x
        return x
    x = L0_attn_x
    x = x + _layernorm(_L0_attn_ref(_layernorm(x, axis=-1), L0_attn_wq, L0_attn_bq, L0_attn_wqc, L0_attn_bqc, L0_attn_wqr, L0_attn_bqr, L0_attn_wkv, L0_attn_bkv, L0_attn_wkr, L0_attn_bkr, L0_attn_wkc, L0_attn_bkc, L0_attn_wv, L0_attn_bv, L0_attn_wo, L0_attn_bo), axis=-1)
    x = x + _layernorm(_L0_ffn_ref(_layernorm(x, axis=-1), L0_ffn_Wqkv, L0_ffn_q_scale, L0_ffn_k_scale, L0_ffn_Wo, L0_ffn_ln_g, L0_ffn_ln_b, L0_ffn_W1, L0_ffn_b1, L0_ffn_W2, L0_ffn_b2), axis=-1)
    return x

_drawn_inputs = setup_inputs


def setup_inputs(seed=0):
    import zlib

    import numpy as np

    out = dict(_drawn_inputs(seed))
    spreads = {'L0_ffn_q_scale': (1.0, 0.6),
     'L0_ffn_k_scale': (1.0, 0.6),
     'L0_ffn_ln_g': (1.0, 0.6),
     'L0_ffn_ln_b': (0.0, 0.8),
     'L0_ffn_b1': (0.0, 0.8),
     'L0_ffn_b2': (0.0, 0.336)}
    factors = {'L0_attn_wqr': 5.623,
     'L0_attn_bqr': 8.0,
     'L0_attn_wkr': 5.255,
     'L0_attn_bkr': 8.0,
     'L0_ffn_W1': 4.568,
     'L0_ffn_W2': 4.43}
    for name, (base, spread) in spreads.items():
        noise = np.random.default_rng([zlib.crc32(name.encode()), seed]).standard_normal(out[name].shape)
        drawn = base * np.exp(spread * noise) if base else spread * noise
        out[name] = jnp.asarray(drawn.astype(out[name].dtype))
    for name, factor in factors.items():
        out[name] = (out[name] * factor).astype(out[name].dtype)
    return out
```

```python
import concourse.bass as bass
from concourse import mybir
from contextlib import ExitStack
import numpy as np

F32 = mybir.dt.float32
BF16 = mybir.dt.bfloat16
ALU = mybir.AluOpType
ACT = mybir.ActivationFunctionType
AX = mybir.AxisListType

P = 128
BATCH, SEQ = 4, 512
TT = SEQ // P
TILES = BATCH * TT
A_HEADS, A_HD, A_DC = 16, 8, 32
DEPTH, HEADS, HD, WIN = 6, 16, 64, 32
PAIRS = HEADS // 2
FFN = 341
CHUNKS = [(0, 128), (128, 128), (256, FFN - 256)]
HALF = PAIRS // 2 * P
LN_EPS = 1e-5
NORM_FLOOR = 1e-24
MASKED = -1e30
COS_SLOTS, SIN_SLOTS = 4, 8
RSQRT_SEED = float(0x5F3759DF)
NEWTON = 11


class Count:

    def __init__(self, ctx, nc, name, per=1, credit=0):
        self.sem = ctx.enter_context(nc.semaphore(name))
        self.per, self.credit = per, credit

    def done(self, rnd, k=0):
        return rnd * self.per + (self.credit + k + 1)


TENSOR_STEPS = [
    ("turn'", 12), ("proj", 0), ("turn'", 13), ("proj", 1), ("proj", 2), ("turn'", 14), ("turn'", 15), ("score'", 3),
    ("pturn'", 2), ("proj", 3), ("mix'", 4), ("turn", 0), ("proj", 4), ("proj", 5), ("mix'", 5), ("pturn'", 3),
    ("proj", 6), ("mix'", 6), ("proj", 7), ("mix'", 7), ("turn", 1), ("proj", 8), ("turn", 2), ("out'", 0),
    ("turn", 3), ("out'", 1), ("score", 0), ("proj", 9), ("out'", 2), ("out'", 3), ("turn", 4), ("xwin", 0),
    ("proj", 10), ("proj", 11), ("turn", 5), ("mean'", 0), ("turn", 6), ("turn", 7), ("proj", 12), ("var'", 0),
    ("score", 1), ("norm'", 0), ("proj", 13), ("turn", 8), ("turn", 9), ("hid'", 0), ("proj", 14), ("pturn", 0),
    ("hid'", 1), ("turn", 10), ("xwin", 1), ("hid'", 2), ("turn", 11), ("xwin", 2), ("down'", 0), ("score", 2),
    ("mix", 0), ("pturn", 1), ("proj", 15), ("mix", 1), ("mix", 2), ("xwin", 3), ("mix", 3),
]
SCALAR_STEPS = [
    ("turn'", 12), ("proj", 0), ("turn'", 13), ("proj", 1), ("turn'", 14), ("turn'", 15), ("proj", 2), ("pturn'", 2),
    ("proj", 3), ("exp'", 3), ("mix'", 4), ("turn", 0), ("proj", 4), ("mix'", 5), ("pturn'", 3), ("proj", 5),
    ("mix'", 6), ("proj", 6), ("mix'", 7), ("turn", 1), ("turn", 2), ("proj", 7), ("proj", 8), ("turn", 3),
    ("proj", 9), ("turn", 4), ("xwin", 0), ("exp", 0), ("turn", 5), ("proj", 10), ("var'", 0), ("turn", 6),
    ("turn", 7), ("proj", 11), ("proj", 12), ("norm'", 0), ("turn", 8), ("turn", 9), ("hid'", 0), ("proj", 13),
    ("hid'", 1), ("pturn", 0), ("turn", 10), ("xwin", 1), ("exp", 1), ("hid'", 2), ("turn", 11), ("xwin", 2),
    ("proj", 14), ("mix", 0), ("pturn", 1), ("proj", 15), ("mix", 1), ("mix", 2), ("xwin", 3), ("mix", 3), ("exp", 2),
]
VECTOR_STEPS = [
    ("shift", 0), ("sum'", 2), ("proj", 0), ("proj", 1), ("nrm", 0), ("score'", 3), ("proj", 2), ("mix'", 4),
    ("sum'", 3), ("proj", 3), ("mix'", 5), ("nrm", 1), ("proj", 4), ("mix'", 6), ("xwin", 0), ("mix'", 7),
    ("proj", 5), ("nrm", 2), ("proj", 6), ("proj", 7), ("nrm", 3), ("proj", 8), ("score", 0), ("xwin", 1),
    ("proj", 9), ("nrm", 4), ("out'", 3), ("sum", 0), ("mean'", 0), ("xwin", 2), ("proj", 10), ("var'", 0),
    ("proj", 11), ("norm'", 0), ("score", 1), ("hid'", 0), ("nrm", 5), ("hid'", 1), ("proj", 12), ("hid'", 2),
    ("proj", 13), ("sum", 1), ("down'", 0), ("proj", 14), ("score", 2), ("mix", 0), ("nrm", 6), ("mix", 1),
    ("xwin", 3), ("proj", 15), ("mix", 2), ("nrm", 7), ("mix", 3),
]
GPSIMD_STEPS = [
    ("proj", 0), ("proj", 1), ("sum'", 2), ("nrm", 0), ("score'", 3), ("proj", 2), ("sum'", 3), ("proj", 3),
    ("nrm", 1), ("proj", 4), ("proj", 5), ("proj", 6), ("proj", 7), ("nrm", 2), ("proj", 8), ("score", 0), ("nrm", 3),
    ("proj", 9), ("nrm", 4), ("sum", 0), ("proj", 10), ("proj", 11), ("score", 1), ("nrm", 5), ("proj", 12),
    ("proj", 13), ("sum", 1), ("proj", 14), ("score", 2), ("nrm", 6), ("proj", 15), ("nrm", 7),
]
LATE = {"turn'", "sum'", "pturn'", "mix'", "score'", "exp'", "out'", "mean'", "var'", "norm'", "hid'", "down'"}
BANK_USES = {"xwin": 1, "turn": 1, "turn'": 1, "pturn": 2, "pturn'": 2}


def bodies(steps, tables, vo):
    early = [s for s in steps if s[0] not in LATE]
    at = steps.index(("mean'", 0)) if vo else 0
    tables, vo = [("tables", 0)] * tables, [("vo", 0)] * vo
    return {"head": tables + vo + early, "steady": steps, "boundary": tables + steps[:at] + vo + steps[at:],
            "tail": [s for s in steps if s[0] in LATE]}


def bank_uses(steps):
    return sum(BANK_USES.get(kind, 0) for kind, _ in steps)


def sandwich_kernel(nc, x, wqr, bqr, wkv, bkv, wkr, bkr, wv, bv, wo, bo, w_qk, w_vt, w_o, qk_scale, w1, w2, ffn_vec,
                    c_ident, c_rope, c_causal, c_headsel, c_band, c_rot, out):
    ctx = ExitStack()
    with ctx:
        def sb(name, shape, dt=F32):
            return ctx.enter_context(nc.sbuf_tensor(name, shape, dt))

        def count(name, per=1, credit=0):
            return Count(ctx, nc, name, per, credit)

        ident = sb("ident", [P, P])
        ident_bf = sb("ident_bf", [P, P], BF16)
        causal = sb("causal", [P, P])
        causal_bf = sb("causal_bf", [P, P], BF16)
        headsel = sb("headsel", [P, A_HEADS])
        band = sb("band", [P, 2, 2 * WIN])
        mean_w = sb("mean_w", [P, P])
        minus_half = sb("minus_half", [P, TILES])
        a_wkv = sb("a_wkv", [P, A_DC])
        a_wv = sb("a_wv", [A_DC, P])
        a_bias = sb("a_bias", [P, 4])
        a_bkv = sb("a_bkv", [A_DC, 1])
        x_tok = sb("x_tok", [P, TILES, P])
        ln_st = sb("ln_st", [P, TILES, 6])
        ln_mv = sb("ln_mv", [P, TILES, 2])
        ln_rs = sb("ln_rs", [P, TILES])
        a_nmax = sb("a_nmax", [P, 16])
        a_sums = sb("a_sums", [P, A_HEADS * TT])
        a_inv = sb("a_inv", [P, A_HEADS * TT])
        w_qk_sb = sb("w_qk_sb", [P, 2 * HEADS * HD])
        w_vt_sb = sb("w_vt_sb", [P, PAIRS, P])
        w_o_sb = sb("w_o_sb", [P, PAIRS, P])
        vo = sb("vo", [P, HEADS, P])
        rot = sb("rot", [P, 4, TT, HD])
        rot_scaled = sb("rot_scaled", [P, 4, TT, HD])
        qk_scale_sb = sb("qk_scale_sb", [P, 4, HD])
        w1_sb = sb("w1_sb", [P, 2 * FFN])
        w2_sb = sb("w2_sb", [P, 3, P])
        vec = sb("vec", [P, 9])
        x_state = sb("x_state", [P, BATCH, SEQ])
        x_shift = sb("x_shift", [P, WIN + SEQ])
        q_hat = sb("q_hat", [P, PAIRS, SEQ])
        k_hat = sb("k_hat", [P, PAIRS, WIN + SEQ])
        x_win = sb("x_win", [P, SEQ // WIN, P])
        x_dup = sb("x_dup", [P, 2, 4, 2, 2, WIN])
        t_cos = sb("t_cos", [P, COS_SLOTS, HALF])
        t_sin = sb("t_sin", [P, SIN_SLOTS, HALF])
        raw = sb("raw", [P, 2, HALF])
        sq = sb("sq", [P, 2, HALF])
        ssum = sb("ssum", [P, 2, HEADS])
        n_half = sb("n_half", [P, HEADS])
        n_tmp = sb("n_tmp", [P, HEADS])
        rnorm = sb("rnorm", [P, 2, HEADS])
        v_sum = sb("v_sum", [P, TT])
        v_half = sb("v_half", [P, TT])
        v_tmp = sb("v_tmp", [P, TT])
        v_rstd = sb("v_rstd", [P, TT])
        prob = sb("prob", [P, 2, PAIRS, 2, 2 * WIN])
        smax = sb("smax", [P, 2, HEADS])
        sinv = sb("sinv", [P, 2, HEADS])
        prob_t = sb("prob_t", [P, 2, PAIRS, P])
        z = sb("z", [P, HEADS, SEQ])
        x1 = sb("x1", [P, SEQ])
        x1_shift = sb("x1_shift", [P, SEQ])
        xc = sb("xc", [P, SEQ])
        xg = sb("xg", [P, SEQ])
        xn = sb("xn", [P, SEQ])
        gate = sb("gate", [P, 3, SEQ])
        hidden = sb("hidden", [P, 3, SEQ])
        xsq = gate[:, 2, :]
        a_prob = z[:, 0:8, :]
        a_pt = z[:, 8:12, :]
        a_qm = z[:, 12:14, :]
        a_q = q_hat[:, 0:4, :]
        a_k = q_hat[:, 4:8, :]
        a_xt = k_hat[:, 0:4, WIN:WIN + SEQ]
        a_o = k_hat[:, 4:8, WIN:WIN + SEQ]
        a_v = x_win
        a_ckv = hidden
        rope = gate[:, 0:2, :]
        a_wq = xg[:, 0:2 * P].rearrange("p (s n) -> p s n", s=2)
        a_wk = xg[:, 2 * P:4 * P].rearrange("p (s n) -> p s n", s=2)
        a_wo, bv_rows, bo_rows = (xn[:, P * n:P * (n + 1)] for n in range(3))
        n_tok = prob_t[:, :, :, :].rearrange("p a c n -> p (a c) n")
        ps_qk = [ctx.enter_context(nc.psum_tensor(f"ps_qk{i}", [P, 512], F32)) for i in range(2)]
        ps_t = [ctx.enter_context(nc.psum_tensor(f"ps_t{i}", [P, 512], F32)) for i in range(2)]
        ps_s = [ctx.enter_context(nc.psum_tensor(f"ps_s{i}", [P, 512], F32)) for i in range(2)]
        ps_z = [ctx.enter_context(nc.psum_tensor(f"ps_z{i}", [P, 512], F32)) for i in range(2)]
        a_ps = [ps_qk[0], ps_qk[1], ps_s[0], ps_s[1]]

        x_in = count("x_in")
        consts_in = count("consts_in")
        set_up = count("set_up")
        casts = count("casts")
        ln_stats = count("ln_stats")
        ln_aggr = count("ln_aggr")
        ln_eps = count("ln_eps")
        ln_rstd = count("ln_rstd")
        ln_out = count("ln_out")
        ln_add = count("ln_add")
        a_turned = count("a_turned")
        a_copied = count("a_copied")
        a_proj = count("a_proj", 5)
        a_rope = count("a_rope", 6)
        a_gelu = count("a_gelu", 3)
        a_vproj = count("a_vproj")
        a_vdone = count("a_vdone")
        a_qmask = count("a_qmask", 4)
        a_scored = count("a_scored", 16, 8)
        a_max = count("a_max", 16)
        a_exp = count("a_exp", 16, 4)
        a_pturn = count("a_pturn", 16, 8)
        a_pcopy_v = count("a_pcopy_v", 12, 3)
        a_pcopy_s = count("a_pcopy_s", 4, 1)
        a_mixed = count("a_mixed", 16, 4)
        a_recip = count("a_recip", 1, 1)
        a_onorm = count("a_onorm", 1, 1)
        a_yout = count("a_yout")
        a_ycopy = count("a_ycopy")

        x_new = count("x_new", 1, 4)
        qk_in = [count(f"qk_in{n}", 16) for n in range(4)]
        vo_in = count("vo_in", 32)
        scale_in = count("scale_in", 16)
        ffn_in = count("ffn_in", 64)
        tables = count("tables", 4)
        vo_made = count("vo_made", 4)
        vo_copied = count("vo_copied", 4, 1)
        shifted = count("shifted", 2)
        duped = count("duped", 4, 1)
        xw_turned = count("xw_turned", 4, 2)
        proj = count("proj", 16, 1)
        copied_raw = count("copied_raw", 16, 2)
        squared = count("squared", 16)
        terms = count("terms", 16, 1)
        summed = count("summed", 16, 2)
        n_newton = count("n_newton", 8 * NEWTON)
        inv_norm = count("inv_norm", 8, 1)
        added = count("added", 16)
        normed = count("normed", 16, 4)
        turned = count("turned", 16, 8)
        bank_copied = count("bank_copied", 0, 2)
        score_begun = count("score_begun", 4)
        scored = count("scored", 4)
        masked = count("masked", 4, 1)
        s_max = count("s_max", 4)
        centered = count("centered", 4)
        exped = count("exped", 4)
        s_sum = count("s_sum", 4)
        s_inv = count("s_inv", 4)
        p_norm = count("p_norm", 4)
        p_turned = count("p_turned", 8, 4)
        mixed = count("mixed", 8)
        z_even = count("z_even", 8, 1)
        z_odd = count("z_odd", 8, 1)
        attn_out = count("attn_out")
        x1_made = count("x1_made")
        x1_shifted = count("x1_shifted", 2)
        mean_made = count("mean_made")
        xc_made = count("xc_made", 1, 1)
        xsq_made = count("xsq_made")
        var_made = count("var_made", 1, 1)
        v_newton = count("v_newton", NEWTON)
        rstd_made = count("rstd_made", 1, 1)
        rstd_rows = count("rstd_rows")
        xg_made = count("xg_made")
        xn_made = count("xn_made", 1, 1)
        hid_made = count("hid_made", 3, 1)
        gelu_made = count("gelu_made", 3)
        hidden_made = count("hidden_made", 3, 1)
        down_made = count("down_made", 1, 1)
        c_turned = count("c_turned")
        c_copied = count("c_copied")
        stored = count("stored")

        block = ctx.enter_context(nc.Block())

        plans = {name: bodies(steps, name == "vector", name in ("tensor", "vector")) for name, steps in
                 (("tensor", TENSOR_STEPS), ("scalar", SCALAR_STEPS), ("vector", VECTOR_STEPS), ("gpsimd", GPSIMD_STEPS))}
        uses = {name: bank_uses(steps) for name, steps in plans["tensor"].items()}
        assert all([s for s in plans["tensor"][n] if s[0] in BANK_USES] == [s for s in plans["scalar"][n] if s[0] in BANK_USES] for n in uses)
        assert all(n % 2 == 0 for n in uses.values())
        N_HEAD, N_STEADY, N_BOUND = (uses[n] for n in ("head", "steady", "boundary"))
        N_LAYER = (BATCH - 1) * N_STEADY + N_BOUND
        N_USES = N_HEAD + (DEPTH - 1) * N_LAYER + (BATCH - 1) * N_STEADY + uses["tail"]

        SET_UP = 5

        def layer_loop(eng, plan, step):
            def run(name, layer, unit, seq, late_layer, late_seq, first_use):
                use = 0
                for s in plan[name]:
                    kind, k = s
                    if kind in LATE:
                        step(late_layer, unit - 1, late_seq, kind.rstrip("'"), k, first_use, use)
                    else:
                        step(layer, unit, seq, kind, k, first_use, use)
                    use += BANK_USES.get(kind, 0)

            def rest_of_layer(layer, first_use):
                with eng.Fori(1, BATCH) as seq:
                    run("steady", layer, layer * BATCH + seq, seq, layer, seq - 1,
                        (seq - 1) * N_STEADY + first_use)

            run("head", 0, 0, 0, None, None, 0)
            with eng.Fori(0, DEPTH - 1) as layer:
                first = layer * N_LAYER + N_HEAD
                rest_of_layer(layer, first)
                run("boundary", layer + 1, (layer + 1) * BATCH, 0, layer, BATCH - 1,
                    first + (BATCH - 1) * N_STEADY)
            last = N_HEAD + (DEPTH - 1) * N_LAYER
            rest_of_layer(DEPTH - 1, last)
            run("tail", None, DEPTH * BATCH, None, DEPTH - 1, BATCH - 1, last + (BATCH - 1) * N_STEADY)

        @block.sync
        def _(sp):
            for b in range(BATCH):
                sp.dma_start(x_tok[:, TT * b:TT * (b + 1), :], x[b].rearrange("(t p) d -> p t d", p=P)).then_inc(x_in.sem, 16)
            for dst, src in ((ident[:, :], c_ident), (rope[:, :, :], c_rope), (causal[:, :], c_causal),
                             (headsel[:, :], c_headsel), (band[:, :, :], c_band), (rot[:, :, :, :], c_rot),
                             (a_wq[:, :, :], wqr), (a_wk[:, :, :], wkr), (a_wkv[:, :], wkv), (a_wv[:, :], wv),
                             (a_wo[:, :], wo), (a_bias[:, 0:2], bqr), (a_bias[:, 2:4], bkr), (a_bkv[:, :], bkv),
                             (bv_rows[:, :], bv.partition_broadcast(P)), (bo_rows[:, :], bo.partition_broadcast(P))):
                sp.dma_start(dst, src).then_inc(consts_in.sem, 16)

            def load_qk(layer, n):
                cols = slice(HALF * n, HALF * (n + 1))
                sp.dma_start(w_qk_sb[:, cols], w_qk[layer, :, cols]).then_inc(qk_in[n].sem, 16)

            def load_vo(layer):
                sp.dma_start(w_vt_sb[:, :, :], w_vt[layer].rearrange("(c p) d -> p c d", p=P)).then_inc(vo_in.sem, 16)
                sp.dma_start(w_o_sb[:, :, :], w_o[layer].rearrange("(c p) d -> p c d", p=P)).then_inc(vo_in.sem, 16)

            def load_scale(layer):
                sp.dma_start(qk_scale_sb[:, :, :], qk_scale[layer].partition_broadcast(P)).then_inc(scale_in.sem, 16)

            def load_ffn(layer):
                sp.dma_start(w1_sb[:, :], w1[layer]).then_inc(ffn_in.sem, 16)
                sp.dma_start(w2_sb[:, 0:2, :], w2[layer, 0:2 * P, :].rearrange("(c p) d -> p c d", p=P)).then_inc(ffn_in.sem, 16)
                sp.dma_start(w2_sb[0:FFN - 2 * P, 2, :], w2[layer, 2 * P:FFN, :]).then_inc(ffn_in.sem, 16)
                sp.dma_start(vec[:, :], ffn_vec[layer]).then_inc(ffn_in.sem, 16)

            for n in range(4):
                load_qk(0, n)
            load_scale(0)
            load_vo(0)
            load_ffn(0)
            with sp.Fori(0, DEPTH - 1) as layer:
                sp.wait_ge(tables.sem, tables.done(layer, 3))
                load_scale(layer + 1)
                sp.wait_ge(vo_made.sem, vo_made.done(layer, 3))
                load_vo(layer + 1)
                for n in range(4):
                    sp.wait_ge(proj.sem, proj.done(layer * BATCH + (BATCH - 1), 12 + n))
                    load_qk(layer + 1, n)
                sp.wait_ge(x_new.sem, x_new.done(layer * BATCH + (BATCH - 1)))
                load_ffn(layer + 1)
            for b in range(BATCH):
                sp.wait_ge(ln_add.sem, 2 * TILES + TT * (b + 1) - TILES)
                sp.dma_start(out[b].rearrange("(t p) d -> p t d", p=P), n_tok[:, TT * b:TT * (b + 1), :]).then_inc(stored.sem, 16)
            sp.wait_ge(stored.sem, 16 * BATCH)

        @block.gpsimd
        def _(pool):
            pool.sem_inc(normed.sem, normed.credit)
            nc.gpsimd.memset(mean_w[:, :], 1.0 / P).then_inc(set_up.sem, 1)
            nc.gpsimd.memset(minus_half[:, :], -0.5).then_inc(set_up.sem, 1)
            nc.gpsimd.memset(x_shift[:, 0:WIN + 1], 0.0).then_inc(set_up.sem, 1)
            nc.gpsimd.memset(x1_shift[:, 0:1], 0.0).then_inc(set_up.sem, 1)
            nc.gpsimd.memset(k_hat[:, :, 0:WIN], 0.0).then_inc(set_up.sem, 1)
            pool.wait_ge(set_up.sem, SET_UP)

            def ln_rsqrt(rnd):
                pool.wait_ge(ln_aggr.sem, TILES * (rnd + 1))
                nc.gpsimd.tensor_scalar(ln_rs[:, :], ln_mv[:, :, 1], LN_EPS, None, ALU.add).then_inc(ln_eps.sem, 1)
                pool.wait_ge(ln_eps.sem, rnd + 1)
                nc.gpsimd.tensor_tensor(ln_rs[:, :], ln_rs[:, :], minus_half[:, :], ALU.pow).then_inc(ln_rstd.sem, 1)

            ln_rsqrt(0)
            pool.wait_ge(consts_in.sem, 16 * 16)
            with pool.Fori(0, BATCH) as b:
                with pool.Fori(0, 4) as hq:
                    grp = b * 4 + hq
                    for j in range(4):
                        if j == 0:
                            pool.wait_ge(a_gelu.sem, a_gelu.done(b, 2))
                        pool.wait_ge(a_scored.sem, a_scored.done(grp, 4 * (j - 1) - 1))
                        nc.gpsimd.tensor_tensor(a_qm[:, j % 2, :], a_q[:, b, :],
                                                headsel[:, bass.ds(hq * 4 + j, 1)].to_broadcast([P, SEQ]), ALU.mult).then_inc(a_qmask.sem, 1)
            ln_rsqrt(1)
            ln_rsqrt(2)

            def step(layer, u, seq, kind, k, first_use, use):
                if kind == "proj":
                    pool.wait_ge(terms.sem, terms.done(u, k))
                    nc.gpsimd.tensor_tensor(t_cos[:, k % COS_SLOTS, :], t_cos[:, k % COS_SLOTS, :], t_sin[:, k % SIN_SLOTS, :], ALU.add).then_inc(added.sem, 1)
                elif kind == "nrm":
                    pool.wait_ge(inv_norm.sem, inv_norm.done(u, k))
                    pool.wait_ge(added.sem, added.done(u, 2 * k + 1))
                    for i in (2 * k, 2 * k + 1):
                        nc.gpsimd.tensor_tensor(t_sin[:, i % SIN_SLOTS, :].rearrange("p (h d) -> p h d", d=HD),
                                                t_cos[:, i % COS_SLOTS, :].rearrange("p (h d) -> p h d", d=HD),
                                                rnorm[:, k % 2, PAIRS * (i % 2):PAIRS * (i % 2 + 1)].unsqueeze(2).to_broadcast([P, PAIRS, HD]),
                                                ALU.mult).then_inc(normed.sem, 1)
                elif kind == "score":
                    pool.wait_ge(s_max.sem, s_max.done(u, k))
                    s = prob[:, k % 2, :, :, :].rearrange("p c e n -> p (c e) n")
                    nc.gpsimd.tensor_tensor(s, s, smax[:, k % 2, :].unsqueeze(2).to_broadcast([P, HEADS, 2 * WIN]), ALU.subtract).then_inc(centered.sem, 1)
                elif kind == "sum":
                    pool.wait_ge(s_inv.sem, s_inv.done(u, k))
                    s = prob[:, k % 2, :, :, :].rearrange("p c e n -> p (c e) n")
                    nc.gpsimd.tensor_tensor(s, s, sinv[:, k % 2, :].unsqueeze(2).to_broadcast([P, HEADS, 2 * WIN]), ALU.mult).then_inc(p_norm.sem, 1)

            layer_loop(pool, plans["gpsimd"], step)
            ln_rsqrt(3)

        @block.scalar
        def _(act):
            for c in (a_exp, a_pcopy_s, copied_raw, bank_copied, z_even, xn_made):
                act.sem_inc(c.sem, c.credit)

            def copy_bank(n, dst):
                act.wait_ge(a_turned.sem, n + 1)
                nc.scalar.activation(dst, ps_t[n % 2][:, :], ACT.Copy).then_inc(a_copied.sem, 1)

            for b in range(BATCH):
                copy_bank(b, a_xt[:, b, :])
            act.wait_ge(consts_in.sem, 16 * 16)
            for b in range(BATCH):
                act.wait_ge(a_proj.sem, a_proj.done(b, 4))
                nc.scalar.activation(a_ckv[0:A_DC, 0, :] if b % 2 == 0 else a_ckv[0:A_DC, 1, :], ps_z[0][0:A_DC, :], ACT.Gelu,
                                     bias=a_bkv[:, 0:1]).then_inc(a_gelu.sem, 1)
                for n, dst in ((0, a_q), (1, a_k)):
                    act.wait_ge(a_rope.sem, a_rope.done(b, 3 * n + 2))
                    nc.scalar.activation(dst[:, b, :], t_cos[:, n, :], ACT.Gelu).then_inc(a_gelu.sem, 1)
            with act.Fori(0, BATCH) as b:
                act.wait_ge(a_recip.sem, a_recip.done(b, -1))
                with act.Fori(0, 4) as hq:
                    grp = b * 4 + hq
                    for n in range(16 + 4):
                        if n < 16:
                            j, qt = n // 4, n % 4
                            slot = 4 * (j % 2) + qt
                            act.wait_ge(a_max.sem, a_max.done(grp, n))
                            act.wait_ge(a_pturn.sem, a_pturn.done(grp, n - 8))
                            nc.scalar.activation(a_prob[:, slot, 0:P * (qt + 1)], a_ps[qt][:, 0:P * (qt + 1)], ACT.Exp,
                                                 bias=a_nmax[:, n:n + 1],
                                                 accum_out=a_sums[:, bass.ds(hq * 16 + n, 1)]).then_inc(a_exp.sem, 1)
                        m = n - 4
                        if m >= 0 and m % 4 == 3:
                            act.wait_ge(a_pturn.sem, a_pturn.done(grp, m))
                            act.wait_ge(a_mixed.sem, a_mixed.done(grp, m - 4))
                            nc.scalar.activation(a_pt[:, m % 4, :], ps_t[m % 2][:, :], ACT.Copy).then_inc(a_pcopy_s.sem, 1)
            for b in range(BATCH):
                copy_bank(BATCH + b, a_xt[:, b, :])

            def step(layer, u, seq, kind, k, first_use, use):
                def bank(n, dst, src=None):
                    bk = ps_t[(use + n) % 2]
                    nc.scalar.activation(dst, bk[:, :].rearrange("p (c n) -> p c n", n=P), ACT.Copy).then_inc(bank_copied.sem, 1)

                if kind == "xwin":
                    act.wait_ge(xw_turned.sem, xw_turned.done(u, k))
                    bank(0, x_win[:, 4 * k:4 * k + 4, :])
                elif kind == "proj":
                    act.wait_ge(proj.sem, proj.done(u, k))
                    act.wait_ge(summed.sem, summed.done(u, k - 2))
                    nc.scalar.activation(raw[:, k % 2, :], ps_qk[k % 2][:, :], ACT.Copy).then_inc(copied_raw.sem, 1)
                    act.wait_ge(copied_raw.sem, copied_raw.done(u, k))
                    nc.scalar.activation(sq[:, k % 2, :], raw[:, k % 2, :], ACT.Square).then_inc(squared.sem, 1)
                elif kind == "turn":
                    act.wait_ge(turned.sem, turned.done(u, k))
                    t, which, half = k // 4, (k % 4) // 2, k % 2
                    if which == 0:
                        dst = q_hat[:, 4 * half:4 * half + 4, P * t:P * (t + 1)]
                    else:
                        dst = k_hat[:, 4 * half:4 * half + 4, WIN + P * t:WIN + P * (t + 1)]
                    bank(0, dst)
                elif kind == "exp":
                    act.wait_ge(centered.sem, centered.done(u, k))
                    nc.scalar.activation(prob[:, k % 2, :, :, :], prob[:, k % 2, :, :, :], ACT.Exp).then_inc(exped.sem, 1)
                elif kind == "pturn":
                    for n in range(2):
                        act.wait_ge(p_turned.sem, p_turned.done(u, 2 * k + n))
                        bank(n, prob_t[:, k % 2, 4 * n:4 * n + 4, :])
                elif kind == "mix":
                    act.wait_ge(mixed.sem, mixed.done(u, k))
                    zo = z[:, :, 64 * k:64 * k + 64].rearrange("p (c e) (w n) -> p e w c n", e=2, w=2)
                    nc.scalar.activation(zo[:, 0], ps_z[0][:, :].rearrange("p (w c n) -> p w c n", w=2, n=WIN), ACT.Copy).then_inc(z_even.sem, 1)
                elif kind == "var":
                    act.wait_ge(xc_made.sem, xc_made.done(u))
                    act.wait_ge(var_made.sem, var_made.done(u, -1))
                    nc.scalar.activation(xsq[:, :], xc[:, :], ACT.Square).then_inc(xsq_made.sem, 1)
                elif kind == "norm":
                    act.wait_ge(ffn_in.sem, ffn_in.done(layer, 63))
                    act.wait_ge(xg_made.sem, xg_made.done(u))
                    act.wait_ge(hid_made.sem, hid_made.done(u, -1))
                    nc.scalar.activation(xn[:, :], xg[:, :], ACT.Identity, bias=vec[:, 1:2]).then_inc(xn_made.sem, 1)
                elif kind == "hid":
                    rows = CHUNKS[k][1]
                    act.wait_ge(hid_made.sem, hid_made.done(u, k))
                    act.wait_ge(hidden_made.sem, hidden_made.done(u, -1))
                    nc.scalar.activation(gate[0:rows, k, :], ps_z[1][0:rows, :], ACT.Gelu, bias=vec[0:rows, 5 + k:6 + k]).then_inc(gelu_made.sem, 1)

            layer_loop(act, plans["scalar"], step)

        @block.vector
        def _(dve):
            for c in (a_pcopy_v, a_onorm, a_recip, duped, terms, vo_copied, summed, inv_norm, rstd_made, masked, z_odd, xc_made, hidden_made):
                dve.sem_inc(c.sem, c.credit)

            def layer_norm(rnd, src, dst):
                dve.wait_ge(ln_out.sem, TILES * rnd)
                for i in range(TILES):
                    nc.vector.bn_stats(ln_st[:, i, :], src[:, i, :]).then_inc(ln_stats.sem, 1)
                dve.wait_ge(ln_stats.sem, TILES * (rnd + 1))
                for i in range(TILES):
                    nc.vector.bn_aggr(ln_mv[:, i, :], ln_st[:, i, :]).then_inc(ln_aggr.sem, 1)
                dve.wait_ge(ln_rstd.sem, rnd + 1)
                for i in range(TILES):
                    nc.vector.tensor_scalar(dst[:, i, :], src[:, i, :], ln_mv[:, i, 0:1], ln_rs[:, i:i + 1],
                                            ALU.subtract, ALU.mult).then_inc(ln_out.sem, 1)

            dve.wait_ge(x_in.sem, 16 * BATCH)
            layer_norm(0, x_tok, n_tok)
            dve.wait_ge(consts_in.sem, 16 * 16)
            nc.vector.tensor_copy(ident_bf[:, :], ident[:, :]).then_inc(casts.sem, 1)
            nc.vector.tensor_copy(causal_bf[:, :], causal[:, :]).then_inc(casts.sem, 1)
            for b in range(BATCH):
                for n in range(2):
                    for sw, buf in ((0, t_cos), (1, t_sin)):
                        dve.wait_ge(a_proj.sem, a_proj.done(b, 2 * n + sw))
                        if b:
                            dve.wait_ge(a_gelu.sem, a_gelu.done(b - 1, 1 + n))
                        nc.vector.scalar_tensor_tensor(out=buf[:, n, :], in0=a_ps[2 * n + sw][:, :],
                                                       scalar=a_bias[:, 2 * n + sw:2 * n + sw + 1], in1=rope[:, sw, :],
                                                       op0=ALU.add, op1=ALU.mult).then_inc(a_rope.sem, 1)
                    dve.wait_ge(a_rope.sem, a_rope.done(b, 3 * n + 1))
                    nc.vector.tensor_tensor(t_cos[:, n, :], t_cos[:, n, :], t_sin[:, n, :], ALU.add).then_inc(a_rope.sem, 1)
                dve.wait_ge(a_vproj.sem, b + 1)
                nc.vector.tensor_tensor(a_v[:, TT * b:TT * (b + 1), :], ps_z[1][:, :].rearrange("p (t d) -> p t d", d=P),
                                        bv_rows[:, :].unsqueeze(1).to_broadcast([P, TT, P]), ALU.add).then_inc(a_vdone.sem, 1)
            with dve.Fori(0, BATCH) as b:
                with dve.Fori(0, 4) as hq:
                    grp = b * 4 + hq
                    for n in range(16 + 4):
                        if n < 16:
                            qt = n % 4
                            dve.wait_ge(a_scored.sem, a_scored.done(grp, n))
                            nc.vector.tensor_reduce(a_nmax[:, n:n + 1], a_ps[qt][:, 0:P * (qt + 1)], AX.X, ALU.max, negate=True).then_inc(a_max.sem, 1)
                        m = n - 4
                        if m >= 0 and m % 4 != 3:
                            w = P * (m % 4 + 1)
                            dve.wait_ge(a_pturn.sem, a_pturn.done(grp, m))
                            dve.wait_ge(a_mixed.sem, a_mixed.done(grp, m - 4))
                            nc.vector.tensor_copy(a_pt[:, m % 4, 0:w], ps_t[m % 2][:, 0:w]).then_inc(a_pcopy_v.sem, 1)
                dve.wait_ge(a_mixed.sem, a_mixed.done(b * 4 + 3, 15))
                dve.wait_ge(a_onorm.sem, a_onorm.done(b, -1))
                nc.vector.reciprocal(a_inv[:, :], a_sums[:, :]).then_inc(a_recip.sem, 1)
                dve.wait_ge(a_recip.sem, a_recip.done(b))
                nc.vector.tensor_tensor(a_o[:, b, :].rearrange("p (q h d) -> p q h d", q=TT, d=A_HD),
                                        ps_z[0][:, :].rearrange("p (q h d) -> p q h d", q=TT, d=A_HD),
                                        a_inv[:, :].rearrange("p (h q) -> p q h", q=TT).unsqueeze(3).to_broadcast([P, TT, A_HEADS, A_HD]),
                                        ALU.mult).then_inc(a_onorm.sem, 1)
            for b in range(BATCH):
                dve.wait_ge(a_yout.sem, b + 1)
                nc.vector.tensor_tensor(n_tok[:, TT * b:TT * (b + 1), :], a_ps[b][:, :].rearrange("p (t d) -> p t d", d=P),
                                        bo_rows[:, :].unsqueeze(1).to_broadcast([P, TT, P]), ALU.add).then_inc(a_ycopy.sem, 1)
            dve.wait_ge(a_ycopy.sem, BATCH)
            layer_norm(1, n_tok, n_tok)
            dve.wait_ge(ln_out.sem, 2 * TILES)
            for b in range(BATCH):
                s = slice(TT * b, TT * (b + 1))
                nc.vector.tensor_tensor(x_tok[:, s, :], x_tok[:, s, :], n_tok[:, s, :], ALU.add).then_inc(ln_add.sem, TT)
            dve.wait_ge(ln_add.sem, TILES)
            layer_norm(2, x_tok, n_tok)
            for b in range(BATCH):
                dve.wait_ge(a_turned.sem, 2 * BATCH + b + 1)
                nc.vector.tensor_copy(x_state[:, b, :], ps_t[b % 2][:, :]).then_inc(x_new.sem, 1)

            def inverse_sqrt(x, half, tmp, y, newton, rnd, first, made):
                n = [first]

                def after():
                    dve.wait_ge(newton.sem, newton.done(rnd, n[0]))
                    n[0] += 1

                int_y = y.bitcast(mybir.dt.int32)
                after()
                nc.vector.tensor_scalar(int_y, x.bitcast(mybir.dt.int32), 1, None, ALU.logical_shift_right).then_inc(newton.sem, 1)
                after()
                nc.vector.tensor_scalar(int_y, int_y, -1.0, RSQRT_SEED, ALU.mult, ALU.add).then_inc(newton.sem, 1)
                nc.vector.tensor_scalar(half[:, :], x, -0.5, None, ALU.mult)
                for last in (False, False, True):
                    after()
                    nc.vector.tensor_tensor(tmp[:, :], y, y, ALU.mult).then_inc(newton.sem, 1)
                    after()
                    nc.vector.tensor_tensor(tmp[:, :], tmp[:, :], half[:, :], ALU.mult).then_inc(newton.sem, 1)
                    after()
                    ins = nc.vector.scalar_tensor_tensor(out=y, in0=tmp[:, :], scalar=1.5, in1=y, op0=ALU.add, op1=ALU.mult)
                    ins.then_inc((made if last else newton).sem, 1)
                assert n[0] == first + NEWTON

            def step(layer, u, seq, kind, k, first_use, use):
                if kind == "tables":
                    dve.wait_ge(scale_in.sem, scale_in.done(layer, 15))
                    dve.wait_ge(terms.sem, terms.done(u, -1))
                    for n in range(4):
                        nc.vector.tensor_tensor(rot_scaled[:, n, :, :], rot[:, n, :, :],
                                                qk_scale_sb[:, n, :].unsqueeze(1).to_broadcast([P, TT, HD]), ALU.mult).then_inc(tables.sem, 1)
                    dve.wait_ge(tables.sem, tables.done(layer, 3))
                elif kind == "vo":
                    for r in range(2):
                        for e in range(2):
                            dve.wait_ge(vo_made.sem, vo_made.done(layer, 2 * r + e))
                            nc.vector.tensor_copy(vo[:, :, :].rearrange("p (c e) d -> p e c d", e=2)[:, e, 4 * r:4 * r + 4, :],
                                                  ps_s[e][:, :].rearrange("p (c d) -> p c d", d=P)).then_inc(vo_copied.sem, 1)
                elif kind == "shift":
                    dve.wait_ge(x_new.sem, x_new.done(u, -4))
                    dve.wait_ge(proj.sem, proj.done(u, -1))
                    dve.wait_ge(duped.sem, duped.done(u, -1))
                    nc.vector.tensor_copy(x_shift[0:64, WIN:], x_state[0:64, seq, :]).then_inc(shifted.sem, 1)
                    nc.vector.tensor_copy(x_shift[64:P, WIN + 1:], x_state[64:P, seq, 0:SEQ - 1]).then_inc(shifted.sem, 1)
                elif kind == "xwin":
                    if k == 0:
                        dve.wait_ge(shifted.sem, shifted.done(u, 1))
                    dve.wait_ge(xw_turned.sem, xw_turned.done(u, k - 2))
                    for a in range(2):
                        at = WIN * (4 * k + a)
                        ins = nc.vector.tensor_copy(x_dup[:, k % 2, :, :, a, :], x_shift[:, at:at + 4 * WIN].rearrange("p (w n) -> p w n", n=WIN)
                                                    .unsqueeze(2).to_broadcast([P, 4, 2, WIN]))
                    ins.then_inc(duped.sem, 1)
                elif kind == "proj":
                    t, which = k // 4, (k % 4) // 2
                    dve.wait_ge(copied_raw.sem, copied_raw.done(u, k))
                    dve.wait_ge(turned.sem, turned.done(u, k - SIN_SLOTS))
                    dve.wait_ge(normed.sem, normed.done(u, k - COS_SLOTS))
                    src = raw[:, k % 2, :].rearrange("p (h a d) -> p h a d", a=2, d=HD // 2)
                    for n, buf, s in ((0, t_cos[:, k % COS_SLOTS, :], src), (1, t_sin[:, k % SIN_SLOTS, :], src[:, :, ::-1, :])):
                        table = rot_scaled[:, 2 * which + n, t, :].rearrange("p (a d) -> p a d", a=2)
                        ins = nc.vector.tensor_tensor(buf.rearrange("p (h a d) -> p h a d", a=2, d=HD // 2), s,
                                                      table.unsqueeze(1).to_broadcast([P, PAIRS, 2, HD // 2]), ALU.mult)
                    ins.then_inc(terms.sem, 1)
                    dve.wait_ge(squared.sem, squared.done(u, k))
                    dve.wait_ge(inv_norm.sem, inv_norm.done(u, k // 2 - 2))
                    nc.vector.tensor_reduce(ssum[:, k // 2 % 2, PAIRS * (k % 2):PAIRS * (k % 2 + 1)],
                                            sq[:, k % 2, :].rearrange("p (h d) -> p h d", d=HD), AX.X, ALU.add).then_inc(summed.sem, 1)
                elif kind == "nrm":
                    dve.wait_ge(summed.sem, summed.done(u, 2 * k + 1))
                    dve.wait_ge(inv_norm.sem, inv_norm.done(u, k - 1))
                    dve.wait_ge(normed.sem, normed.done(u, 2 * k - 3))
                    slot = ssum[:, k % 2, :]
                    nc.vector.tensor_scalar(slot, slot, NORM_FLOOR, None, ALU.max).then_inc(n_newton.sem, 1)
                    inverse_sqrt(slot, n_half, n_tmp, rnorm[:, k % 2, :], n_newton, u, NEWTON * k, inv_norm)
                elif kind == "score":
                    dve.wait_ge(scored.sem, scored.done(u, k))
                    dve.wait_ge(p_turned.sem, p_turned.done(u, 2 * k - 3))
                    for e in range(2):
                        ins = nc.vector.tensor_tensor(prob[:, k % 2, :, e, :], ps_s[e][:, :].rearrange("p (c n) -> p c n", n=2 * WIN),
                                                      band[:, 0 if k == 0 else 1, :].unsqueeze(1).to_broadcast([P, PAIRS, 2 * WIN]), ALU.add)
                    ins.then_inc(masked.sem, 1)
                    dve.wait_ge(masked.sem, masked.done(u, k))
                    nc.vector.tensor_reduce(smax[:, k % 2, :], prob[:, k % 2, :, :, :].rearrange("p c e n -> p (c e) n"), AX.X, ALU.max).then_inc(s_max.sem, 1)
                elif kind == "sum":
                    dve.wait_ge(exped.sem, exped.done(u, k))
                    nc.vector.tensor_reduce(sinv[:, k % 2, :], prob[:, k % 2, :, :, :].rearrange("p c e n -> p (c e) n"), AX.X, ALU.add).then_inc(s_sum.sem, 1)
                    dve.wait_ge(s_sum.sem, s_sum.done(u, k))
                    nc.vector.reciprocal(sinv[:, k % 2, :], sinv[:, k % 2, :]).then_inc(s_inv.sem, 1)
                elif kind == "mix":
                    dve.wait_ge(mixed.sem, mixed.done(u, k))
                    zo = z[:, :, 64 * k:64 * k + 64].rearrange("p (c e) (w n) -> p e w c n", e=2, w=2)
                    nc.vector.tensor_copy(zo[:, 1], ps_z[1][:, :].rearrange("p (w c n) -> p w c n", w=2, n=WIN)).then_inc(z_odd.sem, 1)
                elif kind == "out" and k == 3:
                    dve.wait_ge(attn_out.sem, attn_out.done(u))
                    nc.vector.tensor_tensor(x1[:, :], ps_z[0][:, :], x_state[:, seq, :], ALU.add).then_inc(x1_made.sem, 1)
                    dve.wait_ge(x1_made.sem, x1_made.done(u))
                    dve.wait_ge(xc_made.sem, xc_made.done(u, -1))
                    nc.vector.tensor_copy(x1_shift[0:64, :], x1[0:64, :]).then_inc(x1_shifted.sem, 1)
                    nc.vector.tensor_copy(x1_shift[64:P, 1:], x1[64:P, 0:SEQ - 1]).then_inc(x1_shifted.sem, 1)
                elif kind == "mean":
                    dve.wait_ge(mean_made.sem, mean_made.done(u))
                    nc.vector.tensor_tensor(xc[:, :], x1_shift[:, :], ps_z[1][:, :], ALU.subtract).then_inc(xc_made.sem, 1)
                elif kind == "var":
                    dve.wait_ge(var_made.sem, var_made.done(u))
                    dve.wait_ge(rstd_made.sem, rstd_made.done(u, -1))
                    nc.vector.tensor_scalar(v_sum[:, :], ps_z[0][:, 0:TT], LN_EPS, None, ALU.add).then_inc(v_newton.sem, 1)
                    inverse_sqrt(v_sum[:, :], v_half, v_tmp, v_rstd[:, :], v_newton, u, 0, rstd_made)
                elif kind == "norm":
                    dve.wait_ge(ffn_in.sem, ffn_in.done(layer, 63))
                    dve.wait_ge(rstd_rows.sem, rstd_rows.done(u))
                    dve.wait_ge(xn_made.sem, xn_made.done(u, -1))
                    nc.vector.scalar_tensor_tensor(out=xg[:, :], in0=xc[:, :], scalar=vec[:, 0:1], in1=ps_z[0][:, :],
                                                   op0=ALU.mult, op1=ALU.mult).then_inc(xg_made.sem, 1)
                elif kind == "hid":
                    rows = CHUNKS[k][1]
                    dve.wait_ge(gelu_made.sem, gelu_made.done(u, k))
                    dve.wait_ge(down_made.sem, down_made.done(u, -1))
                    nc.vector.scalar_tensor_tensor(out=hidden[0:rows, k, :], in0=ps_z[0][0:rows, :], scalar=vec[0:rows, 2 + k:3 + k],
                                                   in1=gate[0:rows, k, :], op0=ALU.add, op1=ALU.mult).then_inc(hidden_made.sem, 1)
                elif kind == "down":
                    dve.wait_ge(down_made.sem, down_made.done(u))
                    nc.vector.scalar_tensor_tensor(out=x_state[:, seq, :], in0=ps_z[0][:, :], scalar=vec[:, 8:9], in1=x1[:, :],
                                                   op0=ALU.add, op1=ALU.add).then_inc(x_new.sem, 1)
                    dve.wait_ge(x_new.sem, x_new.done(u))

            layer_loop(dve, plans["vector"], step)
            for b in range(BATCH):
                dve.wait_ge(c_turned.sem, b + 1)
                nc.vector.tensor_copy(n_tok[:, TT * b:TT * (b + 1), :], ps_t[b % 2][:, :].rearrange("p (t d) -> p t d", d=P)).then_inc(c_copied.sem, 1)
            dve.wait_ge(c_copied.sem, BATCH)
            layer_norm(3, n_tok, n_tok)
            dve.wait_ge(ln_out.sem, 4 * TILES)
            for b in range(BATCH):
                s = slice(TT * b, TT * (b + 1))
                nc.vector.tensor_tensor(n_tok[:, s, :], x_tok[:, s, :], n_tok[:, s, :], ALU.add).then_inc(ln_add.sem, TT)

        @block.tensor
        def _(pe):
            for c in (a_scored, a_pturn, a_mixed, proj, xw_turned, turned, p_turned, var_made, hid_made, down_made):
                pe.sem_inc(c.sem, c.credit)
            pe.wait_ge(consts_in.sem, 16 * 16)
            pe.wait_ge(casts.sem, 2)
            pe.wait_ge(set_up.sem, SET_UP)

            def turn_tiles(n, src, ready, sem):
                for t in range(TT):
                    ins = nc.tensor.transpose(ps_t[n % 2][:, P * t:P * (t + 1)], src(t), ident[:, :])
                ins.then_inc(sem, 1)

            for b in range(BATCH):
                pe.wait_ge(ln_out.sem, TT * (b + 1))
                if b >= 2:
                    pe.wait_ge(a_copied.sem, b - 1)
                turn_tiles(b, lambda t: n_tok[:, TT * b + t, :], None, a_turned.sem)
            for b in range(BATCH):
                pe.wait_ge(a_copied.sem, b + 1)
                for n, w in enumerate((a_wq, a_wk)):
                    for sw in range(2):
                        if b:
                            pe.wait_ge(a_rope.sem, a_rope.done(b - 1, 3 * n + sw))
                        nc.tensor.matmul(a_ps[2 * n + sw][:, :], w[:, sw, :], a_xt[:, b, :], start=True, stop=True).then_inc(a_proj.sem, 1)
                if b:
                    pe.wait_ge(a_gelu.sem, a_gelu.done(b - 1, 0))
                nc.tensor.matmul(ps_z[0][0:A_DC, :], a_wkv[:, :], a_xt[:, b, :], start=True, stop=True).then_inc(a_proj.sem, 1)
                pe.wait_ge(a_gelu.sem, a_gelu.done(b, 0))
                pe.wait_ge(a_vdone.sem, b)
                for t in range(TT):
                    ins = nc.tensor.matmul(ps_z[1][:, P * t:P * (t + 1)], a_ckv[0:A_DC, b % 2, P * t:P * (t + 1)], a_wv[:, :], start=True, stop=True)
                ins.then_inc(a_vproj.sem, 1)
            pe.wait_ge(a_gelu.sem, a_gelu.done(BATCH - 1, 2))
            pe.wait_ge(a_vdone.sem, BATCH)
            with pe.Fori(0, BATCH) as b:
                with pe.Fori(0, 4) as hq:
                    grp = b * 4 + hq
                    for n in range(16 + 5):
                        if n < 16:
                            j, qt = n // 4, n % 4
                            if qt == 0:
                                pe.wait_ge(a_qmask.sem, a_qmask.done(grp, j))
                            pe.wait_ge(a_exp.sem, a_exp.done(grp, n - 4))
                            nc.tensor.matmul(a_ps[qt][:, 0:P * (qt + 1)], a_qm[:, j % 2, P * qt:P * (qt + 1)],
                                             a_k[:, b, 0:P * (qt + 1)], start=True, stop=False, skip_group_check=True)
                            nc.tensor.matmul(a_ps[qt][:, P * qt:P * (qt + 1)], ident_bf[:, :], causal_bf[:, :],
                                             start=False, stop=True, skip_group_check=True).then_inc(a_scored.sem, 1)
                        m = n - 4
                        if 0 <= m < 16:
                            qt, slot = m % 4, 4 * (m // 4 % 2) + m % 4
                            pe.wait_ge(a_exp.sem, a_exp.done(grp, m))
                            if (m - 2) % 4 == 3:
                                pe.wait_ge(a_pcopy_s.sem, a_pcopy_s.done(grp, (m - 2) // 4))
                            else:
                                pe.wait_ge(a_pcopy_v.sem, a_pcopy_v.done(grp, 3 * ((m - 2) // 4) + (m - 2) % 4))
                            for kb in range(qt + 1):
                                ins = nc.tensor.transpose(ps_t[m % 2][:, P * kb:P * (kb + 1)], a_prob[:, slot, P * kb:P * (kb + 1)], ident[:, :])
                            ins.then_inc(a_pturn.sem, 1)
                        m = n - 5
                        if m >= 0:
                            qt = m % 4
                            if qt == 3:
                                pe.wait_ge(a_pcopy_s.sem, a_pcopy_s.done(grp, m // 4))
                            else:
                                pe.wait_ge(a_pcopy_v.sem, a_pcopy_v.done(grp, 3 * (m // 4) + qt))
                            if m == 0:
                                pe.wait_ge(a_onorm.sem, a_onorm.done(b, -1))
                            col = (hq * 4 + m // 4) * A_HD
                            for kb in range(qt + 1):
                                ins = nc.tensor.matmul(ps_z[0][:, bass.ds(col + P * qt, A_HD)], a_pt[:, m % 4, P * kb:P * (kb + 1)],
                                                       a_v[:, b * TT + kb, bass.ds(col, A_HD)], start=(kb == 0), stop=(kb == qt))
                            ins.then_inc(a_mixed.sem, 1)
            pe.wait_ge(a_onorm.sem, a_onorm.done(BATCH, -1))
            for b in range(BATCH):
                pe.wait_ge(a_copied.sem, BATCH + max(b - 1, 0))
                turn_tiles(b, lambda t: a_o[:, b, P * t:P * (t + 1)], None, a_turned.sem)
            for b in range(BATCH):
                pe.wait_ge(a_copied.sem, BATCH + b + 1)
                for t in range(TT):
                    ins = nc.tensor.matmul(a_ps[b][:, P * t:P * (t + 1)], a_xt[:, b, P * t:P * (t + 1)], a_wo[:, :], start=True, stop=True)
                ins.then_inc(a_yout.sem, 1)
            for b in range(BATCH):
                pe.wait_ge(ln_out.sem, 2 * TILES + TT * (b + 1))
                if b >= 2:
                    pe.wait_ge(x_new.sem, b - 1)
                turn_tiles(b, lambda t: n_tok[:, TT * b + t, :], None, a_turned.sem)
            pe.wait_ge(x_new.sem, 4)

            def step(layer, u, seq, kind, k, first_use, use):
                def copied(n):
                    pe.wait_ge(bank_copied.sem, first_use + (bank_copied.credit + n))

                if kind == "vo":
                    pe.wait_ge(vo_in.sem, vo_in.done(layer, 31))
                    pe.wait_ge(masked.sem, masked.done(u, -1 if use == 0 else 0))
                    for r in range(2):
                        for e in range(2):
                            pe.wait_ge(vo_copied.sem, vo_copied.done(layer, 2 * r + e - 2) if r else vo_copied.done(layer, -1))
                            for c in range(4):
                                ins = nc.tensor.matmul(ps_s[e][:, P * c:P * (c + 1)], w_vt_sb[64 * e:64 * e + 64, 4 * r + c, :],
                                                       w_o_sb[64 * e:64 * e + 64, 4 * r + c, :], start=True, stop=True)
                            ins.then_inc(vo_made.sem, 1)
                    pe.wait_ge(vo_copied.sem, vo_copied.done(layer, 3))
                elif kind == "xwin":
                    pe.wait_ge(duped.sem, duped.done(u, k))
                    copied(use - 1)
                    for w in range(4):
                        ins = nc.tensor.transpose(ps_t[use % 2][:, P * w:P * (w + 1)],
                                                  x_dup[:, k % 2, w, :, :, :].rearrange("p e a n -> p (e a n)"), ident[:, :])
                    ins.then_inc(xw_turned.sem, 1)
                elif kind == "proj":
                    t, col = k // 4, (k % 4) * HALF
                    if k == 0:
                        pe.wait_ge(shifted.sem, shifted.done(u, 1))
                    if k < 4:
                        pe.wait_ge(qk_in[k].sem, qk_in[k].done(layer, 15))
                    pe.wait_ge(copied_raw.sem, copied_raw.done(u, k - 2))
                    nc.tensor.matmul(ps_qk[k % 2][:, :], x_shift[:, WIN + P * t:WIN + P * (t + 1)], w_qk_sb[:, col:col + HALF],
                                     start=True, stop=True).then_inc(proj.sem, 1)
                elif kind == "turn":
                    pe.wait_ge(normed.sem, normed.done(u, k))
                    copied(use - 1)
                    for c in range(4):
                        ins = nc.tensor.transpose(ps_t[use % 2][:, P * c:P * (c + 1)], t_sin[:, k % SIN_SLOTS, P * c:P * (c + 1)], ident[:, :])
                    ins.then_inc(turned.sem, 1)
                elif kind == "score":
                    copied(use)
                    pe.wait_ge(masked.sem, masked.done(u, k - 1))
                    pe.sem_inc(score_begun.sem, 1)
                    for c in range(TT):
                        at = P * k + WIN * c
                        for p in range(PAIRS):
                            for e in range(2):
                                rows = slice(64 * e, 64 * e + 64)
                                ins = nc.tensor.matmul(ps_s[e][WIN * c:WIN * (c + 1), 2 * WIN * p:2 * WIN * (p + 1)],
                                                       q_hat[rows, p, at:at + WIN], k_hat[rows, p, at:at + 2 * WIN], start=True, stop=True)
                    ins.then_inc(scored.sem, 1)
                elif kind == "pturn":
                    pe.wait_ge(p_norm.sem, p_norm.done(u, k))
                    for n in range(2):
                        copied(use + n - 1)
                        for c in range(4):
                            ins = nc.tensor.transpose(ps_t[(use + n) % 2][:, P * c:P * (c + 1)],
                                                      prob[:, k % 2, 4 * n + c, :, :].rearrange("p e n -> p (e n)"), ident[:, :])
                        ins.then_inc(p_turned.sem, 1)
                elif kind == "mix":
                    copied(use)
                    if k == 0:
                        pe.wait_ge(x_new.sem, x_new.done(u, -1))
                    pe.wait_ge(z_even.sem, z_even.done(u, k - 1))
                    pe.wait_ge(z_odd.sem, z_odd.done(u, k - 1))
                    for w in range(2):
                        c = 2 * (k % 2) + w
                        for e in range(2):
                            rows = slice(64 * e, 64 * e + 64)
                            ins = nc.tensor.matmul(ps_z[e][:, PAIRS * WIN * w:PAIRS * WIN * (w + 1)], x_win[rows, 2 * k + w, :],
                                                   prob_t[rows, k // 2 % 2, :, WIN * c:WIN * (c + 1)], start=True, stop=True)
                    ins.then_inc(mixed.sem, 1)
                elif kind == "out":
                    if k == 0:
                        pe.wait_ge(z_even.sem, z_even.done(u, 7))
                        pe.wait_ge(z_odd.sem, z_odd.done(u, 7))
                    for h in range(4 * k, 4 * k + 4):
                        ins = nc.tensor.matmul(ps_z[0][:, :], vo[:, h, :], z[:, h, :], start=(h == 0), stop=(h == HEADS - 1))
                    if k == 3:
                        ins.then_inc(attn_out.sem, 1)
                elif kind == "mean":
                    pe.wait_ge(x1_shifted.sem, x1_shifted.done(u, 1))
                    nc.tensor.matmul(ps_z[1][:, :], mean_w[:, :], x1_shift[:, :], start=True, stop=True).then_inc(mean_made.sem, 1)
                elif kind == "var":
                    pe.wait_ge(xsq_made.sem, xsq_made.done(u))
                    for t in range(TT):
                        ins = nc.tensor.matmul(ps_z[0][:, t:t + 1], xsq[:, P * t:P * (t + 1)], mean_w[:, 0:1], start=True, stop=True)
                    ins.then_inc(var_made.sem, 1)
                elif kind == "norm":
                    pe.wait_ge(rstd_made.sem, rstd_made.done(u))
                    for t in range(TT):
                        ins = nc.tensor.matmul(ps_z[0][:, P * t:P * (t + 1)], v_rstd[:, t:t + 1].to_broadcast([P, P]), ident[:, :],
                                               start=True, stop=True)
                    ins.then_inc(rstd_rows.sem, 1)
                elif kind == "hid":
                    lo, rows = CHUNKS[k]
                    if k == 0:
                        pe.wait_ge(ffn_in.sem, ffn_in.done(layer, 63))
                        pe.wait_ge(xn_made.sem, xn_made.done(u))
                    else:
                        pe.wait_ge(hidden_made.sem, hidden_made.done(u, k - 1))
                    nc.tensor.matmul(ps_z[1][0:rows, :], w1_sb[:, FFN + lo:FFN + lo + rows], xn[:, :], start=True, stop=True)
                    nc.tensor.matmul(ps_z[0][0:rows, :], w1_sb[:, lo:lo + rows], xn[:, :], start=True, stop=True).then_inc(hid_made.sem, 1)
                elif kind == "down":
                    pe.wait_ge(hidden_made.sem, hidden_made.done(u, 2))
                    for n, (lo, rows) in enumerate(CHUNKS):
                        ins = nc.tensor.matmul(ps_z[0][:, :], w2_sb[0:rows, n, :], hidden[0:rows, n, :], start=(n == 0), stop=(n == 2))
                    ins.then_inc(down_made.sem, 1)

            layer_loop(pe, plans["tensor"], step)
            pe.wait_ge(x_new.sem, 4 + DEPTH * BATCH)
            pe.wait_ge(bank_copied.sem, bank_copied.credit + N_USES)
            for b in range(BATCH):
                if b >= 2:
                    pe.wait_ge(c_copied.sem, b - 1)
                turn_tiles(b, lambda t: x_state[:, b, P * t:P * (t + 1)], None, c_turned.sem)


def constants():
    f = np.float32
    one = f(1.0)
    inv = (one / f(10000.0) ** (np.arange(0, P, 2, dtype=f) / f(P))).astype(f)
    ang = np.arange(SEQ, dtype=f)[:, None] * inv[None, :]
    ang = np.concatenate([ang, ang], -1).astype(f)
    sign = np.where(np.arange(P) < P // 2, -1.0, 1.0).astype(f)
    c_rope = np.stack([np.cos(ang).T, np.sin(ang).T * sign[:, None]], 1).astype(f)
    causal = np.where(np.arange(P)[None, :] > np.arange(P)[:, None], MASKED, 0.0).astype(f)
    headsel = np.where(np.arange(P)[:, None] // A_HD == np.arange(A_HEADS)[None, :], 1.0 / np.sqrt(A_HD), 0.0).astype(f)
    q, k = np.arange(P)[:, None] % WIN, np.arange(2 * WIN)[None, :]
    band = np.where((k > q + WIN) | (k < q), MASKED, 0.0)
    first = np.where((np.arange(P)[:, None] < WIN) & (k < WIN), MASKED, band)
    c_band = np.stack([first, band], 1).astype(f)
    half = np.arange(0, HD, 2, dtype=f)
    inv = (one / f(10000.0) ** (half / f(HD))).astype(f)
    t = np.arange(SEQ, dtype=f)
    ang = (t[:, None] * inv[None, :]).astype(f)
    ang = np.concatenate([ang, ang], -1)
    base = ((half + f(0.4 * HD)) / f(1.4 * HD)).astype(f)
    scale = (base[None, :] ** ((t - SEQ // 2) / f(WIN // 2))[:, None]).astype(f)
    scale = np.concatenate([scale, scale], -1)
    sign = np.where(np.arange(HD) < HD // 2, -1.0, 1.0).astype(f)
    cos, sin = np.cos(ang), np.sin(ang) * sign
    tabs = np.stack([cos * scale * f(8.0), sin * scale * f(8.0), cos * (one / scale), sin * (one / scale)], 0).astype(f)
    c_rot = tabs.reshape(4, TT, P, HD).transpose(2, 0, 1, 3)
    return [np.eye(P, dtype=f), c_rope, causal, headsel, c_band, np.ascontiguousarray(c_rot)]


def layout(inputs):
    g = {k: np.asarray(v) for k, v in inputs.items()}
    a = {k[len("L0_attn_"):]: v for k, v in g.items() if k.startswith("L0_attn_")}
    w = {k[len("L0_ffn_"):]: v for k, v in g.items() if k.startswith("L0_ffn_")}
    swap = np.r_[P // 2:P, 0:P // 2]
    inner = HEADS * HD
    vec = np.zeros((DEPTH, P, 9), np.float32)
    vec[:, :, 0], vec[:, :, 1], vec[:, :, 8] = w["ln_g"], w["ln_b"], w["b2"]
    for n, (lo, rows) in enumerate(CHUNKS):
        vec[:, :rows, 2 + n] = w["b1"][:, lo:lo + rows]
        vec[:, :rows, 5 + n] = w["b1"][:, FFN + lo:FFN + lo + rows]
    hswap = np.r_[HD // 2:HD, 0:HD // 2]
    return [
        a["x"],
        np.stack([a["wqr"], a["wqr"][:, swap]], 1), np.stack([a["bqr"], a["bqr"][swap]], 1),
        a["wkv"], a["bkv"].reshape(A_DC, 1),
        np.stack([a["wkr"], a["wkr"][:, swap]], 1), np.stack([a["bkr"], a["bkr"][swap]], 1),
        a["wv"], a["bv"], a["wo"], a["bo"],
        w["Wqkv"][:, :, 0:2 * inner],
        w["Wqkv"][:, :, 2 * inner:].transpose(0, 2, 1),
        w["Wo"],
        np.stack([w["q_scale"], w["q_scale"][:, hswap], w["k_scale"], w["k_scale"][:, hswap]], 1),
        w["W1"], w["W2"], vec,
    ]


def kernel(**inputs):
    import concourse.bacc as _bacc
    from concourse.bass_utils import run_bass_kernel_spmd as _run

    nc = _bacc.Bacc("TRN2", target_bir_lowering=False, num_devices=1)
    arrays, args = {}, []
    for i, a in enumerate(layout(inputs) + constants()):
        name = f"in_{i}_dram"
        arrays[name] = np.ascontiguousarray(a)
        args.append(nc.dram_tensor(name, a.shape, mybir.dt.from_np(a.dtype), kind="ExternalInput").ap())
    args.append(nc.dram_tensor("out_0_dram", (BATCH, SEQ, P), F32, kind="ExternalOutput").ap())
    sandwich_kernel(nc, *args)
    r = _run(nc, [arrays], core_ids=[0])
    return r.results[0]["out_0_dram"]
```
